# Optimizing a Trainium2 kernel written in Bass

```python
import numpy as np
import jax
import jax.numpy as jnp

def _softmax(x, axis=-1):
    return jax.nn.softmax(x, axis=axis)

def _gelu(x):
    return jax.nn.gelu(x, approximate=True)

def _silu(x):
    return jax.nn.silu(x)

def _sigmoid(x):
    return jax.nn.sigmoid(x)

def _layernorm(x, axis=-1, eps=1e-05):
    m = jnp.mean(x, axis=axis, keepdims=True)
    v = jnp.var(x, axis=axis, keepdims=True)
    return (x - m) / jnp.sqrt(v + eps)

def _scatter_add(tgt, idx, src, axis=0):
    return tgt.at[idx].add(src)

def _segment_sum(src, seg, n):
    return jax.ops.segment_sum(src, seg, n)
kernel_name = 'mk_dlrm_tower_d1_rec_r8_f54a12'

def setup_inputs(seed: int=0):
    np.random.seed(seed)
    _w = jnp.asarray

    def _rec_inputs():
        import jax
        import jax.numpy as jnp
        _tk = jax.random.key(seed)
        ids = jnp.stack([jax.random.randint(jax.random.fold_in(_tk, 200 + f), (2048,), 0, v, jnp.int32) for f, v in enumerate([12500, 125000, 1000, 1250, 1000, 1000, 12500, 12500, 12500, 1000, 1250, 1000, 1000, 1000, 1250, 12500, 1000, 12500, 1250, 125000, 125000, 1250, 1000, 1000, 1250, 1250])], axis=1)
        tbl_0 = 0.05 * jax.random.normal(jax.random.fold_in(_tk, 500 + 0), (12500, 64), jnp.float32)
        tbl_1 = 0.05 * jax.random.normal(jax.random.fold_in(_tk, 500 + 1), (125000, 64), jnp.float32)
        tbl_2 = 0.05 * jax.random.normal(jax.random.fold_in(_tk, 500 + 2), (1000, 64), jnp.float32)
        tbl_3 = 0.05 * jax.random.normal(jax.random.fold_in(_tk, 500 + 3), (1250, 64), jnp.float32)
        tbl_4 = 0.05 * jax.random.normal(jax.random.fold_in(_tk, 500 + 4), (1000, 64), jnp.float32)
        tbl_5 = 0.05 * jax.random.normal(jax.random.fold_in(_tk, 500 + 5), (1000, 64), jnp.float32)
        tbl_6 = 0.05 * jax.random.normal(jax.random.fold_in(_tk, 500 + 6), (12500, 64), jnp.float32)
        tbl_7 = 0.05 * jax.random.normal(jax.random.fold_in(_tk, 500 + 7), (12500, 64), jnp.float32)
        tbl_8 = 0.05 * jax.random.normal(jax.random.fold_in(_tk, 500 + 8), (12500, 64), jnp.float32)
        tbl_9 = 0.05 * jax.random.normal(jax.random.fold_in(_tk, 500 + 9), (1000, 64), jnp.float32)
        tbl_10 = 0.05 * jax.random.normal(jax.random.fold_in(_tk, 500 + 10), (1250, 64), jnp.float32)
        tbl_11 = 0.05 * jax.random.normal(jax.random.fold_in(_tk, 500 + 11), (1000, 64), jnp.float32)
        tbl_12 = 0.05 * jax.random.normal(jax.random.fold_in(_tk, 500 + 12), (1000, 64), jnp.float32)
        tbl_13 = 0.05 * jax.random.normal(jax.random.fold_in(_tk, 500 + 13), (1000, 64), jnp.float32)
        tbl_14 = 0.05 * jax.random.normal(jax.random.fold_in(_tk, 500 + 14), (1250, 64), jnp.float32)
        tbl_15 = 0.05 * jax.random.normal(jax.random.fold_in(_tk, 500 + 15), (12500, 64), jnp.float32)
        tbl_16 = 0.05 * jax.random.normal(jax.random.fold_in(_tk, 500 + 16), (1000, 64), jnp.float32)
        tbl_17 = 0.05 * jax.random.normal(jax.random.fold_in(_tk, 500 + 17), (12500, 64), jnp.float32)
        tbl_18 = 0.05 * jax.random.normal(jax.random.fold_in(_tk, 500 + 18), (1250, 64), jnp.float32)
        tbl_19 = 0.05 * jax.random.normal(jax.random.fold_in(_tk, 500 + 19), (125000, 64), jnp.float32)
        tbl_20 = 0.05 * jax.random.normal(jax.random.fold_in(_tk, 500 + 20), (125000, 64), jnp.float32)
        tbl_21 = 0.05 * jax.random.normal(jax.random.fold_in(_tk, 500 + 21), (1250, 64), jnp.float32)
        tbl_22 = 0.05 * jax.random.normal(jax.random.fold_in(_tk, 500 + 22), (1000, 64), jnp.float32)
        tbl_23 = 0.05 * jax.random.normal(jax.random.fold_in(_tk, 500 + 23), (1000, 64), jnp.float32)
        tbl_24 = 0.05 * jax.random.normal(jax.random.fold_in(_tk, 500 + 24), (1250, 64), jnp.float32)
        tbl_25 = 0.05 * jax.random.normal(jax.random.fold_in(_tk, 500 + 25), (1250, 64), jnp.float32)
        _rk = jax.random.fold_in(_tk, 7)
        r_dense_t = 7.22013e-05 + 1.00017 * jax.random.normal(jax.random.fold_in(_rk, 101), (2048, 256), jnp.float32)
        W_top1 = 0.0360844 * jax.random.normal(jax.random.fold_in(_tk, 801), (768, 512), jnp.float32)
        W_top2 = 0.0441942 * jax.random.normal(jax.random.fold_in(_tk, 802), (512, 256), jnp.float32)
        W_top3 = 0.0625 * jax.random.normal(jax.random.fold_in(_tk, 803), (256, 1), jnp.float32)
        b_top1 = jnp.zeros((512,), jnp.float32)
        b_top2 = jnp.zeros((256,), jnp.float32)
        return (r_dense_t, ids, tbl_0, tbl_1, tbl_2, tbl_3, tbl_4, tbl_5, tbl_6, tbl_7, tbl_8, tbl_9, tbl_10, tbl_11, tbl_12, tbl_13, tbl_14, tbl_15, tbl_16, tbl_17, tbl_18, tbl_19, tbl_20, tbl_21, tbl_22, tbl_23, tbl_24, tbl_25, W_top1, b_top1, W_top2, b_top2, W_top3)
    r_dense_t, ids, tbl_0, tbl_1, tbl_2, tbl_3, tbl_4, tbl_5, tbl_6, tbl_7, tbl_8, tbl_9, tbl_10, tbl_11, tbl_12, tbl_13, tbl_14, tbl_15, tbl_16, tbl_17, tbl_18, tbl_19, tbl_20, tbl_21, tbl_22, tbl_23, tbl_24, tbl_25, W_top1, b_top1, W_top2, b_top2, W_top3 = _rec_inputs()

    def _L0_rec_setup():
        import jax, jax.numpy as jnp
        import numpy as np
        EPS = 1e-05
        NI = 33
        TRIL_I, TRIL_J = np.tril_indices(NI, k=-1)

        def layer_norm(x, g, b):
            m = jnp.mean(x, axis=-1, keepdims=True)
            v = jnp.mean(jnp.square(x - m), axis=-1, keepdims=True)
            return (x - m) * jax.lax.rsqrt(v + EPS) * g + b
        key = jax.random.key(seed)
        ks = jax.random.split(key, 8)
        B, D_DENSE, N_SP, D_SP = (4096, 256, 26, 64)
        E, PROJ, MAXD, NFLAT = (128, 32, 512, 528)
        dense_t = jax.random.normal(ks[0], (B, D_DENSE), dtype=jnp.float32)
        sparse_t = jax.random.normal(ks[1], (B, N_SP, D_SP), dtype=jnp.float32)
        Wd = jax.random.normal(ks[2], (E, D_DENSE), dtype=jnp.float32) / np.sqrt(D_DENSE)
        Ws = jax.random.normal(ks[3], (E, D_SP), dtype=jnp.float32) / np.sqrt(D_SP)
        Wsi = jax.random.normal(ks[4], (PROJ, N_SP), dtype=jnp.float32) / np.sqrt(N_SP)
        Wl = jax.random.normal(ks[5], (MAXD, NFLAT), dtype=jnp.float32) / np.sqrt(NFLAT)
        gd = jnp.ones((E,), jnp.float32)
        bd = jnp.zeros((E,), jnp.float32)
        gs = jnp.ones((E,), jnp.float32)
        bs = jnp.zeros((E,), jnp.float32)
        gsi = jnp.ones((PROJ,), jnp.float32)
        bsi = jnp.zeros((PROJ,), jnp.float32)
        gl = jnp.ones((MAXD,), jnp.float32)
        bl = jnp.zeros((MAXD,), jnp.float32)
        return {'dense_t': dense_t, 'sparse_t': sparse_t, 'Wd': Wd, 'gd': gd, 'bd': bd, 'Ws': Ws, 'gs': gs, 'bs': bs, 'Wsi': Wsi, 'gsi': gsi, 'bsi': bsi, 'Wl': Wl, 'gl': gl, 'bl': bl, 'dims_in_use': 384}
    _L0_rec_all = _L0_rec_setup()
    _L0_rec_in = {k: v for k, v in _L0_rec_all.items() if k in ('Wd', 'gd', 'bd', 'Ws', 'gs', 'bs', 'Wsi', 'gsi', 'bsi', 'Wl', 'gl', 'bl')}
    del _L0_rec_all
    return {'r_dense_t': r_dense_t, 'ids': ids, 'tbl_0': tbl_0, 'tbl_1': tbl_1, 'tbl_2': tbl_2, 'tbl_3': tbl_3, 'tbl_4': tbl_4, 'tbl_5': tbl_5, 'tbl_6': tbl_6, 'tbl_7': tbl_7, 'tbl_8': tbl_8, 'tbl_9': tbl_9, 'tbl_10': tbl_10, 'tbl_11': tbl_11, 'tbl_12': tbl_12, 'tbl_13': tbl_13, 'tbl_14': tbl_14, 'tbl_15': tbl_15, 'tbl_16': tbl_16, 'tbl_17': tbl_17, 'tbl_18': tbl_18, 'tbl_19': tbl_19, 'tbl_20': tbl_20, 'tbl_21': tbl_21, 'tbl_22': tbl_22, 'tbl_23': tbl_23, 'tbl_24': tbl_24, 'tbl_25': tbl_25, 'W_top1': W_top1, 'b_top1': b_top1, 'W_top2': W_top2, 'b_top2': b_top2, 'W_top3': W_top3, 'L0_rec_Wd': _L0_rec_in['Wd'], 'L0_rec_gd': _L0_rec_in['gd'], 'L0_rec_bd': _L0_rec_in['bd'], 'L0_rec_Ws': _L0_rec_in['Ws'], 'L0_rec_gs': _L0_rec_in['gs'], 'L0_rec_bs': _L0_rec_in['bs'], 'L0_rec_Wsi': _L0_rec_in['Wsi'], 'L0_rec_gsi': _L0_rec_in['gsi'], 'L0_rec_bsi': _L0_rec_in['bsi'], 'L0_rec_Wl': _L0_rec_in['Wl'], 'L0_rec_gl': _L0_rec_in['gl'], 'L0_rec_bl': _L0_rec_in['bl']}

def reference(r_dense_t, ids, tbl_0, tbl_1, tbl_2, tbl_3, tbl_4, tbl_5, tbl_6, tbl_7, tbl_8, tbl_9, tbl_10, tbl_11, tbl_12, tbl_13, tbl_14, tbl_15, tbl_16, tbl_17, tbl_18, tbl_19, tbl_20, tbl_21, tbl_22, tbl_23, tbl_24, tbl_25, W_top1, b_top1, W_top2, b_top2, W_top3, L0_rec_Wd, L0_rec_gd, L0_rec_bd, L0_rec_Ws, L0_rec_gs, L0_rec_bs, L0_rec_Wsi, L0_rec_gsi, L0_rec_bsi, L0_rec_Wl, L0_rec_gl, L0_rec_bl):
    import jax
    import jax.numpy as jnp

    def _L0_rec_ref(dense_t, sparse_t, Wd, gd, bd, Ws, gs, bs, Wsi, gsi, bsi, Wl, gl, bl, dims_in_use):
        import jax, jax.numpy as jnp
        import numpy as np
        EPS = 1e-05
        NI = 33
        TRIL_I, TRIL_J = np.tril_indices(NI, k=-1)

        def layer_norm(x, g, b):
            m = jnp.mean(x, axis=-1, keepdims=True)
            v = jnp.mean(jnp.square(x - m), axis=-1, keepdims=True)
            return (x - m) * jax.lax.rsqrt(v + EPS) * g + b
        x = layer_norm(dense_t @ Wd.T, gd, bd)
        y = layer_norm(jnp.einsum('bnd,ed->bne', sparse_t, Ws), gs, bs)
        y = jnp.einsum('bne,pn->bep', y, Wsi)
        y = layer_norm(y, gsi, bsi)
        y = jnp.swapaxes(y, 1, 2)
        T = jnp.concatenate([x[:, None, :], y], axis=1)
        Z = jnp.einsum('bnd,bmd->bnm', T, T)
        Zflat = Z[:, TRIL_I, TRIL_J]
        out = layer_norm(Zflat @ Wl.T, gl, bl)
        maxd = out.shape[-1]
        mask = (jnp.arange(maxd) < dims_in_use).astype(out.dtype)
        return out * mask
    e = jnp.stack([tbl_0[ids[:, 0]], tbl_1[ids[:, 1]], tbl_2[ids[:, 2]], tbl_3[ids[:, 3]], tbl_4[ids[:, 4]], tbl_5[ids[:, 5]], tbl_6[ids[:, 6]], tbl_7[ids[:, 7]], tbl_8[ids[:, 8]], tbl_9[ids[:, 9]], tbl_10[ids[:, 10]], tbl_11[ids[:, 11]], tbl_12[ids[:, 12]], tbl_13[ids[:, 13]], tbl_14[ids[:, 14]], tbl_15[ids[:, 15]], tbl_16[ids[:, 16]], tbl_17[ids[:, 17]], tbl_18[ids[:, 18]], tbl_19[ids[:, 19]], tbl_20[ids[:, 20]], tbl_21[ids[:, 21]], tbl_22[ids[:, 22]], tbl_23[ids[:, 23]], tbl_24[ids[:, 24]], tbl_25[ids[:, 25]]], axis=1)
    z = _L0_rec_ref(r_dense_t, e, L0_rec_Wd, L0_rec_gd, L0_rec_bd, L0_rec_Ws, L0_rec_gs, L0_rec_bs, L0_rec_Wsi, L0_rec_gsi, L0_rec_bsi, L0_rec_Wl, L0_rec_gl, L0_rec_bl, 384)
    z = z.reshape(z.shape[0], -1)
    h = jnp.concatenate([z, r_dense_t], axis=1)
    h = jnp.maximum(h @ W_top1 + b_top1, 0.0)
    h = jnp.maximum(h @ W_top2 + b_top2, 0.0)
    y = h @ W_top3
    return y

_drawn_inputs = setup_inputs


def setup_inputs(seed=0):
    import zlib

    import numpy as np

    out = dict(_drawn_inputs(seed))
    spreads = {'b_top1': (0.0, 0.1),
     'b_top2': (0.0, 0.1),
     'L0_rec_gd': (1.0, 0.6),
     'L0_rec_bd': (0.0, 0.8),
     'L0_rec_gs': (1.0, 0.6),
     'L0_rec_bs': (0.0, 0.1),
     'L0_rec_gsi': (1.0, 0.2),
     'L0_rec_bsi': (0.0, 0.1),
     'L0_rec_gl': (1.0, 0.2),
     'L0_rec_bl': (0.0, 0.1)}
    factors = {}
    for name, (base, spread) in spreads.items():
        noise = np.random.default_rng([zlib.crc32(name.encode()), seed]).standard_normal(out[name].shape)
        drawn = base * np.exp(spread * noise) if base else spread * noise
        out[name] = jnp.asarray(drawn.astype(out[name].dtype))
    for name, factor in factors.items():
        out[name] = (out[name] * factor).astype(out[name].dtype)
    return out
```

```python
import math
from contextlib import ExitStack

import concourse.bass as bass
from concourse import mybir

FP32 = mybir.dt.float32
INT32 = mybir.dt.int32
ALU = mybir.AluOpType
ACT = mybir.ActivationFunctionType
AXX = mybir.AxisListType.X

P = 128
NF, D = 26, 64
E = 128
NP = 32
DD = 256
MAXD, DIMS = 512, 384
H1, H2 = 512, 256
EPS = 1e-5
NQ = 4
NJ = P // NQ
TPG = 2
GB = TPG * P
GRAM = NP + 2
BATCHES = [range(0, 3), range(3, 6), range(6, 9), range(9, 13)]
MIX_AT = (0, 1, 3, 5)
PIECES = 8

SW = [NP - 8 * q for q in range(4)]
SB = [8 * sum(SW[:q]) for q in range(4)]
ROW_X = 8 * sum(SW)
ROW_S = ROW_X + NP
ROW_SX = ROW_S + NP
ROW_ONE = ROW_SX + 1
RC = 6
LASTK = ROW_ONE + 1 - 5 * P


def tri(i, j):
    return i * (i - 1) // 2 + j


def after(engine, sem, value):
    if not isinstance(value, int) or value > 0:
        engine.wait_ge(sem, value)
        if not isinstance(value, int) and engine.engine in (mybir.EngineType.Activation, mybir.EngineType.Pool, mybir.EngineType.SP):
            engine.nop(nofuse=True)


def tower(nc, a, out):
    T = a["ids"].shape[0] // P
    G = T // TPG
    LAG = 2
    tables = [a[f"tbl_{f}"] for f in range(NF)]

    with ExitStack() as ctx:
        def sb(name, shape, dt=FP32):
            return ctx.enter_context(nc.sbuf_tensor(name, shape, dt))

        def sem(name):
            return ctx.enter_context(nc.semaphore(name))

        ws = sb("ws", [P, D]); wsi = sb("wsi", [NP, NF]); wd = sb("wd", [P, DD])
        gs = sb("gs", [P, 1]); bs = sb("bs", [P, 1]); gd = sb("gd", [P, 1]); bd = sb("bd", [P, 1])
        gsi = sb("gsi", [P, NP]); bsi = sb("bsi", [P, NP]); gl = sb("gl", [P, 3]); bl = sb("bl", [P, 3])
        w1 = sb("w1", [P, 5, H1]); w2 = sb("w2", [P, 4, H2]); w3 = sb("w3", [P, 2])
        b1 = sb("b1", [P, 4]); b2 = sb("b2", [P, 2])
        ident = sb("ident", [P, P]); center = sb("center", [P, P]); center_p = sb("center_p", [NP, NP])
        ones = sb("ones", [P, P]); mean_e = sb("mean_e", [P, P]); mean_o = sb("mean_o", [P, P])
        wsc = sb("wsc", [P, 2, D])
        wsg = sb("wsg", [P, 2, D])
        gram_w = sb("gram_w", [P, P])
        proj = [sb(f"proj{h}", [P, E]) for h in range(2)]
        mix = sb("mix", [P, NQ * NP])
        bias_y = sb("bias_y", [P, NP])
        wdt = sb("wdt", [P, 2, E])
        wlt = sb("wlt", [P, RC, MAXD])
        wtmp = sb("wtmp", [P, 4, 8, NP]); u1 = sb("u1", [P, 4, NP]); u2 = sb("u2", [P, 4, NP])
        wtmp2 = sb("wtmp2", [P, 4, NP])
        gpq = sb("gpq", [P, 8, NP]); wmean = sb("wmean", [P, RC])
        b1p = sb("b1p", [P, 4])
        idx = [sb(f"idx{h}", [P, NF], INT32) for h in range(2)]
        emb = [sb(f"emb{h}", [P, NF, D]) for h in range(2)]
        nrm = [sb(f"nrm{h}", [P, NF, D]) for h in range(2)]
        byn = [sb(f"byn{h}", [P, NJ, D]) for h in range(2)]
        embt = sb("embt", [P, 13, P])
        prod = [sb(f"prod{h}", [P, 8, D]) for h in range(2)]
        var_n = sb("var_n", [P, NF]); var_m = sb("var_m", [P, NF]); std_n = sb("std_n", [P, NF]); rstd_n = sb("rstd_n", [P, NF]); eps = sb("eps", [P, 1])
        mixed = [sb(f"mixed{h}", [P, 512]) for h in range(2)]
        yb = [sb(f"yb{h}", [P, 16, NP]) for h in range(4)]
        sq = [sb(f"sq{h}", [P, 16, NP]) for h in range(2)]
        var_y = [sb(f"var_y{h}", [P, 16]) for h in range(2)]
        std_y = [sb(f"std_y{h}", [P, 16]) for h in range(2)]
        rstd_y = [sb(f"rstd_y{h}", [P, 16]) for h in range(2)]
        V = [sb(f"V{h}", [P, P, GRAM]) for h in range(2)]
        wl = V[0][:, :, :].rearrange("p s c -> p (s c)")[:, 0:4 * 528].rearrange("p (o r) -> p o r", o=4)
        wlr = V[1][:, :, :].rearrange("p s c -> p (s c)")[:, 0:4 * RC * P].rearrange("p (o r) -> p o r", o=4)
        zs = sb("zs", [P, GRAM, TPG, NJ])
        sxr = sb("sxr", [1, NQ, TPG, NJ])
        zt = sb("zt", [P, RC, GB])
        dense = sb("dense", [P, TPG, DD]); dense_l = sb("dense_l", [P, TPG, DD])
        dt = sb("dt", [P, 2, NQ, TPG, NJ]); dtl = sb("dtl", [P, 2, NQ, TPG, NJ])
        sqx = sb("sqx", [P, GB]); sdx = sb("sdx", [P, GB]); rx = sb("rx", [P, GB]); xn = sb("xn", [P, GB]); xt = sb("xt", [P, NQ, TPG, NJ])
        o_sb = sb("o_sb", [P, 4, GB]); sqo = sb("sqo", [P, 4, GB]); sdo = sb("sdo", [P, GB]); ro = sb("ro", [P, GB]); z = sb("z", [P, 3, GB])
        h1 = sb("h1", [P, 4, GB]); h2 = sb("h2", [P, 2, GB]); y_sb = sb("y_sb", [1, NQ, TPG, NJ])

        bank = [ctx.enter_context(nc.psum_tensor(f"bank{i}", [P, 512], FP32)) for i in range(8)]
        b_tr, b_g, b_mix, b_y, b_z, L = bank[0], bank[1], bank[2], bank[3:5], bank[5], bank[6:8]

        by_sample = [nc.dram_tensor(f"by_sample{h}", (NF, P, D), FP32, kind="Internal").ap() for h in range(2)]
        rows = nc.dram_tensor("rows", (ROW_SX + 1, GB), FP32, kind="Internal").ap()

        w_small, w_wl, w_mlp = sem("w_small"), sem("w_wl"), sem("w_mlp")
        ident_ready, consts_ready, const_chain = sem("ident_ready"), sem("consts_ready"), sem("const_chain")
        prep_mm, prep_dve, wlr_act = sem("prep_mm"), sem("prep_dve"), sem("wlr_act")
        idx_loaded = [sem(f"idx_loaded{h}") for h in range(2)]
        gathered = [sem(f"gathered{h}") for h in range(2)]
        emb_transposed, embt_copied, gw_done = sem("emb_transposed"), sem("embt_copied"), sem("gw_done")
        prod_done, varn_done, varm_done, stdn_done, rstdn_done, nrm_ready = (
            sem("prod_done"), sem("varn_done"), sem("varm_done"), sem("stdn_done"), sem("rstdn_done"), sem("nrm_ready"))
        nrm_stored = [sem(f"nrm_stored{h}") for h in range(2)]
        byn_loaded = [sem(f"byn_loaded{h}") for h in range(2)]
        mix_done, mixed_copied, proj_done = sem("mix_done"), sem("mixed_copied"), sem("proj_done")
        y_biased, y_squared, vary_done, stdy_done, rstdy_done, y_scaled = (
            sem("y_biased"), sem("y_squared"), sem("vary_done"), sem("stdy_done"), sem("rstdy_done"), sem("y_scaled"))
        x_in_v = sem("x_in_v")
        gram_done, zs_copied, rows_stored, rows_loaded = sem("gram_done"), sem("zs_copied"), sem("rows_stored"), sem("rows_loaded")
        dense_loaded, densel_loaded = sem("dense_loaded"), sem("densel_loaded")
        x_transposed, dt_copied, x_projected, x_squared, x_var, x_std, x_step, x_ready = (
            sem("x_transposed"), sem("dt_copied"), sem("x_projected"), sem("x_squared"), sem("x_var"), sem("x_std"), sem("x_step"), sem("x_ready"))
        o_done, o_copied, o_squared, o_var, o_std, o_rstd, z_ready = (
            sem("o_done"), sem("o_copied"), sem("o_squared"), sem("o_var"), sem("o_std"), sem("o_rstd"), sem("z_ready"))
        l_transposed, dtl_copied, h1_done, h1_relued, h2_done, h2_relued, y_done, y_copied, out_stored = (
            sem("l_transposed"), sem("dtl_copied"), sem("h1_done"), sem("h1_relued"), sem("h2_done"), sem("h2_relued"),
            sem("y_done"), sem("y_copied"), sem("out_stored"))

        N_SMALL, N_MLP, N_WL = 8, 7, 3
        ids_v = a["ids"].rearrange("(t p) f -> p t f", p=P)
        dense_v = a["r_dense_t"].rearrange("(t p) f -> p t f", p=P)
        out_v = out.rearrange("(g t q j) d -> g q t (j d)", g=G, t=TPG, q=NQ)

        def column(x):
            return x.rearrange("(p o) -> p o", o=1)

        def iterations(engine, body, first=LAG + 2, end=G):
            for i in range(first):
                body(i)
            with engine.Fori(first, end) as i:
                body(i)
            for i in range(end, G + LAG):
                body(i)

        def stages(i):
            if not isinstance(i, int):
                return [(True, True, True)] * TPG, True, True
            live = [tuple(0 <= TPG * i + s - back < T for back in range(3)) for s in range(TPG)]
            return live, i < G, i >= LAG

        def lagging(i, s, k, lag):
            back = 1 if k >= lag else 2
            tile = TPG * i + s - back
            if isinstance(tile, int) and not 0 <= tile < T:
                return None
            return tile, (k - lag) % PIECES, (s - back) % 2

        def wlr_copies(parity):
            for p in range(parity, NP, 2):
                for k in range((p + 7) // 8):
                    n = min(8, p - 8 * k)
                    at = SB[k] + p - 8 * k
                    src = tri(p + 1, 8 * k + 1)
                    yield wlr[:, :, at:at + SW[k] * (n - 1) + 1:SW[k]], wl[:, :, src:src + n]
                yield wlr[:, :, ROW_X + p:ROW_X + p + 1], wl[:, :, tri(p + 1, 0):tri(p + 1, 0) + 1]

        block = ctx.enter_context(nc.Block())

        @block.sync
        def _(sp):
            def load(dst, src, s, slow=False):
                sp.dma_start(dst, src, allow_slow_non_contiguous=slow).then_inc(s, 16)

            for h in range(2):
                load(idx[h][:, :], ids_v[:, h, :], idx_loaded[h])
            load(ws[:, :], a["L0_rec_Ws"], w_small)
            load(gs[:, :], column(a["L0_rec_gs"]), w_small)
            load(bs[:, :], column(a["L0_rec_bs"]), w_small)
            load(wsi[:, :], a["L0_rec_Wsi"], w_small)
            load(wd[:, :], a["L0_rec_Wd"], w_small)
            load(gd[:, :], column(a["L0_rec_gd"]), w_small)
            load(bd[:, :], column(a["L0_rec_bd"]), w_small)
            load(b2[:, :], a["b_top2"].rearrange("(c p) -> p c", p=P), w_small, True)
            load(gl[:, :], a["L0_rec_gl"][0:DIMS].rearrange("(c p) -> p c", p=P), w_mlp, True)
            load(bl[:, :], a["L0_rec_bl"][0:DIMS].rearrange("(c p) -> p c", p=P), w_mlp, True)
            load(b1[:, :], a["b_top1"].rearrange("(c p) -> p c", p=P), w_mlp, True)
            load(w3[:, :], a["W_top3"].rearrange("(c p) o -> p (c o)", p=P), w_mlp, True)
            load(w1[:, 0:3, :], a["W_top1"][0:DIMS, :].rearrange("(c p) m -> p c m", p=P), w_mlp)
            load(w1[:, 3:5, :], a["W_top1"][MAXD:, :].rearrange("(c p) m -> p c m", p=P), w_mlp)
            load(w2[:, :, :], a["W_top2"].rearrange("(c p) m -> p c m", p=P), w_mlp)

            def body(i):
                live, front, back = stages(i)
                for s in range(TPG):
                    t = TPG * i + s
                    if s == 1:
                        if not isinstance(i, int) or i + 1 < G:
                            after(sp, dt_copied, 2 * (i + 1))
                            sp.dma_start(dense[:, :, :], dense_v[:, bass.ds(TPG * (i + 1), TPG), :]).then_inc(dense_loaded, 16)
                        if not isinstance(i, int) or i > LAG:
                            g = i - 1 - LAG
                            after(sp, y_copied, g + 1)
                            sp.dma_start(out_v[bass.ds(g, 1), :, :, :], y_sb[:, :, :, :]).then_inc(out_stored, 16)
                    if live[s][0]:
                        if not isinstance(i, int) or i + 1 < G:
                            after(sp, gathered[s], 16 * NF * (i + 1))
                            sp.dma_start(idx[s][:, :], ids_v[:, bass.ds(t + TPG, 1), :].rearrange("p t f -> p (t f)")).then_inc(idx_loaded[s], 16)
                        after(sp, nrm_ready, t + 1)
                        sp.dma_start(by_sample[s].rearrange("n l d -> l n d"), nrm[s][:, :, :]).then_inc(nrm_stored[s], 16)
                        after(sp, nrm_stored[s], 16 * (i + 1))
                        after(sp, mix_done, 4 * (t - 1))
                        for q in range(NQ):
                            sp.dma_start(byn[s][32 * q:32 * q + NF, :, :],
                                         by_sample[s][:, NJ * q:NJ * (q + 1), :]).then_inc(byn_loaded[s], 16)
                    if s == 1 and (not isinstance(i, int) or 0 <= i + 1 - LAG < G):
                        after(sp, dtl_copied, 2 * (i - LAG + 1))
                        sp.dma_start(dense_l[:, :, :], dense_v[:, bass.ds(TPG * (i + 1 - LAG), TPG), :]).then_inc(densel_loaded, 16)
                    if s == 1 and live[s][2]:
                        g = i - 1
                        after(sp, zs_copied, 5 * TPG * (g + 1))
                        after(sp, rows_loaded, 32 * g)
                        for q in range(NQ):
                            cols = rows[:, 2 * NJ * q:2 * NJ * (q + 1)]
                            for k in range(4):
                                dst = cols[SB[k]:SB[k] + 8 * SW[k], :].rearrange("(i p) c -> p i c", i=8)
                                sp.dma_start(dst, zs[32 * q + 8 * k:32 * q + 32, 8 * k:8 * k + 8, :, :]
                                             .rearrange("p i t j -> p i (t j)")).then_inc(rows_stored, 16)
                            dst = cols[ROW_X:ROW_X + 2 * NP, :].rearrange("(i p) c -> p i c", i=2)
                            sp.dma_start(dst, zs[32 * q:32 * q + 32, NP:NP + 2, :, :].rearrange("p i t j -> p i (t j)")
                                         ).then_inc(rows_stored, 16)
                        sp.dma_start(rows[ROW_SX:ROW_SX + 1, :], sxr[:, :, :, :].rearrange("p q t j -> p (q t j)")
                                     ).then_inc(rows_stored, 16)
                        after(sp, rows_stored, 16 * 21 * (g + 1))
                        after(sp, o_done, 2 * g)
                        sp.dma_start(zt[:, 0:5, :], rows[0:5 * P, :].rearrange("(c k) b -> k c b", k=P)).then_inc(rows_loaded, 16)
                        sp.dma_start(zt[0:ROW_SX + 1 - 5 * P, 5, :], rows[5 * P:ROW_SX + 1, :]).then_inc(rows_loaded, 16)

            sp.dma_start(dense[:, :, :], dense_v[:, 0:TPG, :]).then_inc(dense_loaded, 16)
            iterations(sp, body, end=G - 1)
            sp.wait_ge(y_copied, G)
            sp.dma_start(out_v[G - 1:G, :, :, :], y_sb[:, :, :, :]).then_inc(out_stored, 16)
            sp.wait_ge(out_stored, 16 * G)

        @block.gpsimd
        def _(pool):
            nc.gpsimd.memset(ident[:, :], 0.0).then_inc(ident_ready, 1)
            pool.wait_ge(ident_ready, 1)
            nc.gpsimd.affine_select(out=ident[:, :], in_=ident[:, :], compare_op=ALU.not_equal, fill=1.0, base=0,
                                    pattern=[[-1, P]], channel_multiplier=1).then_inc(ident_ready, 1)

            def body(i):
                for s in range(TPG):
                    t = TPG * i + s
                    after(pool, nrm_ready, t - 1)
                    after(pool, idx_loaded[s], 16 * (i + 1))
                    for f in range(NF):
                        pool.indirect_dma_start(out=emb[s][:, f, :], out_offset=None, in_=tables[f],
                                                in_offset=bass.IndirectOffsetOnAxis(ap=idx[s][:, f:f + 1], axis=0)
                                                ).then_inc(gathered[s], 16)

            for i in range(2):
                body(i)
            with pool.Fori(2, G) as i:
                body(i)

        @block.tensor
        def _(pe):
            pe.wait_ge(w_small, 16 * N_SMALL)
            pe.wait_ge(consts_ready, 1)
            nc.tensor.matmul(bank[0][:, 0:D], center[:, :], ws[:, :], start=True, stop=True).then_inc(prep_mm, 1)
            nc.tensor.matmul(bank[1][0:NF, 0:NP], wsi[:, :], center_p[:, :], start=True, stop=True).then_inc(prep_mm, 1)
            for c in range(2):
                last = nc.tensor.matmul(bank[2][:, c * E:(c + 1) * E], wd[:, c * P:(c + 1) * P], center[:, :], start=True, stop=True)
            last.then_inc(prep_mm, 1)
            pe.wait_ge(w_mlp, 16 * N_MLP)
            for m in range(4):
                for c in range(3):
                    last = nc.tensor.matmul(bank[6][:, m:m + 1], w1[:, c, m * P:(m + 1) * P], bl[:, c:c + 1],
                                            start=(c == 0), stop=(c == 2))
            last.then_inc(prep_mm, 1)
            pe.wait_ge(prep_dve, 1)
            nc.tensor.matmul(bank[3][:, 0:P], wsc[:, :, :].rearrange("p a d -> p (a d)"),
                             wsc[:, :, :].rearrange("p a d -> p (a d)"), start=True, stop=True).then_inc(prep_mm, 1)
            nc.tensor.transpose(bank[4][:, 0:E], wsg[:, :, :].rearrange("p a d -> p (a d)"), ident[:, :]).then_inc(prep_mm, 1)
            pe.wait_ge(prep_dve, 2)
            nc.tensor.matmul(bank[5][:, 0:NP], ones[0:NF, :], mix[0:NF, 0:NP], start=True, stop=True).then_inc(prep_mm, 1)
            pe.wait_ge(prep_dve, 4)

            def prepare_wlt():
                pe.wait_ge(x_step, 2)
                pe.wait_ge(prep_dve, 5)
                for c in range(RC):
                    if c >= 2:
                        pe.wait_ge(prep_dve, 5 + c - 1)
                    for oc in range(4):
                        last = nc.tensor.transpose(L[c % 2][:, oc * P:(oc + 1) * P], wlr[:, oc, c * P:(c + 1) * P], ident[:, :])
                    last.then_inc(prep_mm, 1)
                pe.wait_ge(prep_dve, 5 + RC)

            def slot(i, s, live):
                t = TPG * i + s
                tb, tc = t - 1, t - 2
                sb_, sc = (s + 1) % 2, s
                A, B, C = live
                for k in range(PIECES):
                    if B and k in MIX_AT:
                        g = MIX_AT.index(k)
                        if k == 0:
                            after(pe, byn_loaded[sb_], 64 * (i if s == 1 else i - 1) + 64)
                        after(pe, mixed_copied, 4 * tb + g)
                        for m in range(4):
                            j = 2 * (4 * g + m)
                            last = nc.tensor.matmul(b_mix[:, m * P:(m + 1) * P], byn[sb_][:, j:j + 2, :].rearrange("p j d -> p (j d)"),
                                                    mix[:, :], start=True, stop=True)
                        last.then_inc(mix_done, 1)
                    if A and k < 4:
                        if k == 0:
                            after(pe, gathered[s], 16 * NF * (i + 1))
                        after(pe, embt_copied, 4 * t + k)
                        for n, c in enumerate(BATCHES[k]):
                            last = nc.tensor.transpose(b_tr[:, n * P:(n + 1) * P],
                                                       emb[s][:, 2 * c:2 * c + 2, :].rearrange("p n d -> p (n d)"), ident[:, :])
                        last.then_inc(emb_transposed, 1)
                    if C:
                        if k == 0:
                            after(pe, x_in_v, tc + 1)
                        if k % 2 == 0:
                            after(pe, y_scaled, 8 * tc + k + 2)
                        if k % 2 == 0:
                            after(pe, zs_copied, 5 * tc + k // 2)
                        for jj in range(4):
                            j = 4 * k + jj
                            c0 = GRAM * (j % 8)
                            for q in range(NQ):
                                last = nc.tensor.matmul(b_z[32 * q:32 * q + 32, c0:c0 + GRAM], V[sc][:, 32 * q + j, 0:NP],
                                                        V[sc][:, 32 * q + j, :], start=True, stop=True)
                        if k == 7:
                            last = nc.tensor.matmul(b_z[0:1, 8 * GRAM:8 * GRAM + P], ones[:, 0:1], V[sc][:, :, NP],
                                                    start=True, stop=True)
                        if k % 2:
                            last.then_inc(gram_done, 1)
                    yield k
                    if A and k < 4:
                        after(pe, embt_copied, 4 * t + k + 1)
                        after(pe, prod_done, 4 * t + k)
                        for n, c in enumerate(BATCHES[k]):
                            last = nc.tensor.matmul(b_g[:, n * P:(n + 1) * P], embt[:, c, :], gram_w[:, :], start=True, stop=True)
                        last.then_inc(gw_done, 1)
                    if B:
                        after(pe, mixed_copied, 4 * tb + k // 2 + 1)
                        after(pe, y_biased, 8 * tb + k - 1)
                        nc.tensor.matmul(b_y[k % 2][:, :], proj[k % 2][:, :], mixed[(k // 2) % 2][:, :], start=True, stop=True
                                         ).then_inc(proj_done, 1)

            def body(i):
                live, front, back = stages(i)
                g = i - LAG
                for s in range(TPG):
                    for k in slot(i, s, live[s]):
                        p = PIECES * s + k
                        if p == 0 and (not isinstance(i, int) or i > LAG):
                            output(g - 1)
                        if front and p == 0:
                            after(pe, dense_loaded, 16 * (i + 1))
                            after(pe, h2_relued, 2 * g)
                            for tt in range(TPG):
                                for f in range(2):
                                    n = 2 * tt + f
                                    last = nc.tensor.transpose(L[0][:, n * P:(n + 1) * P], dense[:, tt, f * P:(f + 1) * P], ident[:, :])
                            last.then_inc(x_transposed, 1)
                        if front and p == 2:
                            after(pe, dt_copied, 2 * (i + 1))
                            for f in range(2):
                                last = nc.tensor.matmul(L[0][:, 0:GB], wdt[:, f, :], dt[:, f, :, :, :].rearrange("p q t j -> p (q t j)"),
                                                        start=(f == 0), stop=(f == 1))
                            last.then_inc(x_projected, 1)
                        if front and p == 4:
                            after(pe, x_squared, i + 1)
                            nc.tensor.matmul(L[0][:, GB:2 * GB], mean_e[:, :], sqx[:, :], start=True, stop=True).then_inc(x_var, 1)
                        if back and 4 <= p < 8:
                            oc = p - 4
                            if oc == 0:
                                after(pe, rows_loaded, 32 * (g + 1))
                                after(pe, y_copied, g)
                            if oc == 2:
                                if front:
                                    after(pe, x_step, 2 * (i + 1))
                                else:
                                    after(pe, x_step, 2 * G)
                                    after(pe, h2_relued, 2 * g)
                            for c in range(RC):
                                kk = LASTK if c == RC - 1 else P
                                last = nc.tensor.matmul(L[1 - oc // 2][:, (oc % 2) * GB:(oc % 2 + 1) * GB], wlt[0:kk, c, oc * P:(oc + 1) * P],
                                                        zt[0:kk, c, :], start=(c == 0), stop=(c == RC - 1))
                            if oc % 2:
                                last.then_inc(o_done, 1)
                        if back and p == 9:
                            after(pe, o_squared, 2 * (g + 1))
                            after(pe, o_copied, 2 * (g + 1))
                            for oc in range(4):
                                last = nc.tensor.matmul(L[1][:, 0:GB], mean_o[:, :], sqo[:, oc, :], start=(oc == 0), stop=(oc == 3))
                            last.then_inc(o_var, 1)
                            after(pe, densel_loaded, 16 * (g + 1))
                            for tt in range(TPG):
                                for f in range(2):
                                    n = 2 * tt + f
                                    last = nc.tensor.transpose(L[0][:, n * P:(n + 1) * P], dense_l[:, tt, f * P:(f + 1) * P], ident[:, :])
                            last.then_inc(l_transposed, 1)
                        for m in {11: (0, 1), 12: (2, 3)}.get(p, ()) if back else ():
                            if m == 0:
                                after(pe, dtl_copied, 2 * (g + 1))
                                after(pe, z_ready, g + 1)
                            dst = L[m // 2][:, (m % 2) * GB:(m % 2 + 1) * GB]
                            for n, c in enumerate((3, 4, 0, 1, 2)):
                                rhs = dtl[:, c - 3, :, :, :].rearrange("p q t j -> p (q t j)") if c > 2 else z[:, c, :]
                                last = nc.tensor.matmul(dst, w1[:, c, m * P:(m + 1) * P], rhs, start=(n == 0), stop=(n == 4))
                            if m % 2:
                                last.then_inc(h1_done, 1)
                        if back and p == 14:
                            after(pe, h1_relued, 4 * (g + 1))
                            for m in range(2):
                                for c in range(4):
                                    last = nc.tensor.matmul(L[0][:, m * GB:(m + 1) * GB], w2[:, c, m * P:(m + 1) * P], h1[:, c, :],
                                                            start=(c == 0), stop=(c == 3))
                            last.then_inc(h2_done, 1)
                    if isinstance(i, int) and i == 0 and s == 0:
                        prepare_wlt()

            def output(g):
                after(pe, h2_relued, 2 * (g + 1))
                for c in range(2):
                    last = nc.tensor.matmul(L[1][0:1, 0:GB], w3[:, c:c + 1], h2[:, c, :], start=(c == 0), stop=(c == 1))
                last.then_inc(y_done, 1)

            iterations(pe, body)
            output(G - 1)

        @block.scalar
        def _(act):
            act.dma_start(wl[:, :, :], a["L0_rec_Wl"].rearrange("(c p) r -> p c r", p=P)).then_inc(w_wl, 16)
            act.dma_start(gsi[:, :], a["L0_rec_gsi"].rearrange("(o p) -> o p", o=1).broadcast_to([P, NP])).then_inc(w_wl, 16)
            act.dma_start(bsi[:, :], a["L0_rec_bsi"].rearrange("(o p) -> o p", o=1).broadcast_to([P, NP])).then_inc(w_wl, 16)
            act.wait_ge(const_chain, 1)
            act.wait_ge(w_wl, 16 * N_WL)
            for dst, src in wlr_copies(1):
                last = nc.scalar.activation(dst, src, ACT.Copy)
            last.then_inc(wlr_act, 1)
            act.wait_ge(prep_dve, 4)

            def slot(i, s, live):
                t = TPG * i + s
                tb, tc = t - 1, t - 2
                A, B, C = live
                for k in range(PIECES):
                    if A and k == 4:
                        after(act, varm_done, t + 1)
                        after(act, rstdn_done, t)
                        nc.scalar.activation(std_n[:, :], var_m[:, :], ACT.Sqrt, bias=eps[:, 0:1]).then_inc(stdn_done, 1)
                    if B and k in MIX_AT:
                        g = MIX_AT.index(k)
                        after(act, mix_done, 4 * tb + g + 1)
                        after(act, proj_done, 8 * tb + 2 * g - 2)
                        nc.scalar.activation(mixed[g % 2][:, :], b_mix[:, :], ACT.Copy).then_inc(mixed_copied, 1)
                    if A and k < 4:
                        c0, c1 = BATCHES[k][0], BATCHES[k][-1] + 1
                        after(act, emb_transposed, 4 * t + k + 1)
                        after(act, gw_done, 4 * t + k - 3)
                        nc.scalar.activation(embt[:, c0:c1, :], b_tr[:, 0:(c1 - c0) * P].rearrange("p (c l) -> p c l", l=P),
                                             ACT.Copy).then_inc(embt_copied, 1)
                    if C and k % 2:
                        r = k // 2
                        after(act, gram_done, 4 * tc + r + 1)
                        if r == 0:
                            after(act, rows_stored, 16 * 21 * (i - 1))
                        nc.scalar.activation(zs[:, :, s, 8 * r:8 * r + 8].rearrange("p c j -> p j c"),
                                             b_z[:, 0:8 * GRAM].rearrange("p (j c) -> p j c", c=GRAM), ACT.Copy).then_inc(zs_copied, 1)
                        if r == 3:
                            nc.scalar.activation(sxr[:, :, s, :], b_z[0:1, 8 * GRAM:8 * GRAM + P].rearrange("p (q j) -> p q j", q=NQ),
                                                 ACT.Copy).then_inc(zs_copied, 1)
                    yield k
                    at = lagging(i, s, k, 1)
                    if at:
                        u, n, _ = at
                        after(act, y_biased, 8 * u + n + 1)
                        after(act, vary_done, 8 * u + n - 1)
                        nc.scalar.activation(sq[n % 2][:, :, :], yb[n % 4][:, :, :], ACT.Square, scale=NP ** -0.5
                                             ).then_inc(y_squared, 1)
                    at = lagging(i, s, k, 2)
                    if at:
                        u, n, _ = at
                        after(act, vary_done, 8 * u + n + 1)
                        after(act, rstdy_done, 8 * u + n - 1)
                        nc.scalar.activation(std_y[n % 2][:, :], var_y[n % 2][:, :], ACT.Sqrt, bias=eps[:, 0:1]).then_inc(stdy_done, 1)

            def body(i):
                live, front, back = stages(i)
                g = i - LAG
                for s in range(TPG):
                    for k in slot(i, s, live[s]):
                        p = PIECES * s + k
                        if p == 1 and (not isinstance(i, int) or i > LAG):
                            output(g - 1)
                        if front and p == 1:
                            after(act, x_transposed, i + 1)
                            after(act, x_projected, i)
                            for tt in range(TPG):
                                nc.scalar.activation(dt[:, :, :, tt, :], L[0][:, 2 * tt * P:2 * (tt + 1) * P]
                                                     .rearrange("p (f q j) -> p f q j", f=2, q=NQ), ACT.Copy).then_inc(dt_copied, 1)
                        if front and p == 3:
                            after(act, x_projected, i + 1)
                            after(act, x_var, i)
                            nc.scalar.activation(sqx[:, :], L[0][:, 0:GB], ACT.Square).then_inc(x_squared, 1)
                        if front and p == 4:
                            after(act, x_var, i + 1)
                            after(act, x_step, 2 * i)
                            nc.scalar.activation(sdx[:, :], L[0][:, GB:2 * GB], ACT.Sqrt, bias=eps[:, 0:1]).then_inc(x_std, 1)
                        if back and p in (6, 8):
                            h = (p - 6) // 2
                            after(act, o_done, 2 * g + h + 1)
                            after(act, z_ready, g)
                            after(act, o_var, g)
                            src = L[1 - h][:, :].rearrange("p (c b) -> p c b", c=2)
                            nc.scalar.activation(sqo[:, 2 * h:2 * h + 2, :], src, ACT.Square).then_inc(o_squared, 1)
                            nc.scalar.activation(o_sb[:, 2 * h:2 * h + 2, :], src, ACT.Copy).then_inc(o_copied, 1)
                        if back and p == 9:
                            after(act, o_var, g + 1)
                            after(act, o_rstd, g)
                            nc.scalar.activation(sdo[:, :], L[1][:, 0:GB], ACT.Sqrt, bias=eps[:, 0:1]).then_inc(o_std, 1)
                        if back and p == 10:
                            after(act, l_transposed, g + 1)
                            after(act, h1_done, 2 * g)
                            for tt in range(TPG):
                                nc.scalar.activation(dtl[:, :, :, tt, :], L[0][:, 2 * tt * P:2 * (tt + 1) * P]
                                                     .rearrange("p (f q j) -> p f q j", f=2, q=NQ), ACT.Copy).then_inc(dtl_copied, 1)
                        if back and p in (12, 13):
                            h = p - 12
                            after(act, h1_done, 2 * g + h + 1)
                            after(act, h2_done, g)
                            for m in (2 * h, 2 * h + 1):
                                nc.scalar.activation(h1[:, m, :], L[h][:, (m % 2) * GB:(m % 2 + 1) * GB], ACT.Relu,
                                                     bias=b1p[:, m:m + 1]).then_inc(h1_relued, 1)
                        if back and p == 15:
                            after(act, h2_done, g + 1)
                            after(act, y_done, g)
                            for m in range(2):
                                nc.scalar.activation(h2[:, m, :], L[0][:, m * GB:(m + 1) * GB], ACT.Relu,
                                                     bias=b2[:, m:m + 1]).then_inc(h2_relued, 1)

            def output(g):
                after(act, y_done, g + 1)
                after(act, out_stored, 16 * g)
                nc.scalar.activation(y_sb[:, :, :, :].rearrange("p q t j -> p (q t j)"), L[1][0:1, 0:GB], ACT.Copy).then_inc(y_copied, 1)

            iterations(act, body)
            output(G - 1)

        @block.vector
        def _(dve):
            chain = [0]

            def link(ins):
                chain[0] += 1
                ins.then_inc(const_chain, 1)
                dve.wait_ge(const_chain, chain[0])

            nc.vector.memset(eps[:, :], EPS)
            nc.vector.memset(ones[:, :], 1.0)
            nc.vector.memset(mean_e[:, :], 1.0 / E)
            nc.vector.memset(mean_o[:, :], 1.0 / MAXD)
            for x in (proj[0], proj[1], gram_w, mix):
                nc.vector.memset(x[:, :], 0.0)
            for h in range(2):
                nc.vector.memset(byn[h][:, :, :], 0.0)
            nc.vector.memset(zt[64:96, RC - 1, :], 1.0)
            link(nc.vector.memset(wlr[:, :, :], 0.0))
            dve.wait_ge(ident_ready, 2)
            nc.vector.tensor_scalar(center[:, :], ident[:, :], -1.0 / E, None, ALU.add)
            nc.vector.tensor_scalar(center_p[:, :], ident[0:NP, 0:NP], -1.0 / NP, None, ALU.add).then_inc(consts_ready, 1)
            dve.wait_ge(w_small, 16 * N_SMALL)
            dve.wait_ge(prep_mm, 1)
            for h in range(2):
                nc.vector.tensor_copy(wsc[:, h, :], bank[0][:, 0:D])
                last = nc.vector.tensor_scalar(wsg[:, h, :], bank[0][:, 0:D], gs[:, 0:1], None, ALU.mult)
            last.then_inc(prep_dve, 1)
            dve.wait_ge(prep_mm, 2)
            for q in range(NQ):
                last = nc.vector.tensor_copy(mix[32 * q:32 * q + NF, NP * q:NP * (q + 1)], bank[1][0:NF, 0:NP])
            last.then_inc(prep_dve, 1)
            dve.wait_ge(prep_mm, 4)
            dve.wait_ge(w_mlp, 16 * N_MLP)
            nc.vector.tensor_tensor(b1p[:, :], bank[6][:, 0:4], b1[:, :], ALU.add).then_inc(prep_dve, 1)
            for c in range(3):
                nc.vector.tensor_scalar(w1[:, c, :], w1[:, c, :], gl[:, c:c + 1], None, ALU.mult)
            dve.wait_ge(prep_mm, 3)
            nc.vector.tensor_copy(wdt[:, :, :], bank[2][:, 0:2 * E].rearrange("p (c e) -> p c e", c=2))
            dve.wait_ge(prep_mm, 6)
            for h in range(2):
                r = slice(64 * h, 64 * h + 64)
                nc.vector.tensor_scalar(gram_w[r, r], bank[3][r, r], 1.0 / E, None, ALU.mult)
                nc.vector.tensor_copy(proj[h][r, :], bank[4][r, 0:E])
            dve.wait_ge(prep_mm, 7)
            nc.vector.tensor_scalar(bias_y[:, :], bank[5][:, 0:NP], bs[:, 0:1], None, ALU.mult).then_inc(prep_dve, 1)
            dve.wait_ge(w_wl, 16 * N_WL)
            for dst, src in wlr_copies(0):
                last = nc.vector.tensor_copy(dst, src)
            link(last)
            dve.wait_ge(wlr_act, 1)

            def strip(k):
                return wlr[:, :, SB[k]:SB[k] + 8 * SW[k]].rearrange("o c (i p) -> o c i p", i=8)

            def over(x, k, axis):
                v = x[:, 8 * k:8 * k + 8].unsqueeze(2) if axis == 0 else x[:, 8 * k:NP].unsqueeze(1)
                return v.unsqueeze(1).broadcast_to([P, 4, 8, SW[k]])

            for k in range(4):
                tmp = wtmp[:, :, :, 0:SW[k]]
                link(nc.vector.tensor_tensor(tmp, strip(k), over(bsi, k, 1), ALU.mult))
                link(nc.vector.tensor_reduce(u2[:, :, 8 * k:8 * k + 8], tmp, AXX, ALU.add))
            link(nc.vector.tensor_tensor(wtmp[:, :, 0, :], u2[:, :, :], bsi[:, :].unsqueeze(1).broadcast_to([P, 4, NP]), ALU.mult))
            link(nc.vector.tensor_reduce(wlr[:, :, ROW_ONE:ROW_ONE + 1], wtmp[:, :, 0, :], AXX, ALU.add))
            link(nc.vector.tensor_scalar(wlr[:, :, ROW_ONE:ROW_ONE + 1], wlr[:, :, ROW_ONE:ROW_ONE + 1], float(E), None, ALU.mult))
            for k in range(4):
                tmp = wtmp[:, :, :, 0:SW[k]]
                link(nc.vector.tensor_tensor(tmp, strip(k), over(bsi, k, 0), ALU.mult))
                link(nc.vector.tensor_reduce(u1[:, :, 8 * k:NP] if k == 0 else wtmp2[:, :, 0:SW[k]], tmp.rearrange("o c i p -> o c p i"), AXX, ALU.add))
                if k:
                    link(nc.vector.tensor_tensor(u1[:, :, 8 * k:NP], u1[:, :, 8 * k:NP], wtmp2[:, :, 0:SW[k]], ALU.add))
            link(nc.vector.tensor_tensor(u1[:, :, :], u1[:, :, :], u2[:, :, :], ALU.add))
            gp = gsi[:, :].unsqueeze(1).broadcast_to([P, 4, NP])
            link(nc.vector.tensor_tensor(wlr[:, :, ROW_S:ROW_S + NP], u1[:, :, :], gp, ALU.mult))
            wx = wlr[:, :, ROW_X:ROW_X + NP]
            link(nc.vector.tensor_tensor(wtmp[:, :, 0, :], wx, bsi[:, :].unsqueeze(1).broadcast_to([P, 4, NP]), ALU.mult))
            link(nc.vector.tensor_reduce(wlr[:, :, ROW_SX:ROW_SX + 1], wtmp[:, :, 0, :], AXX, ALU.add))
            link(nc.vector.tensor_tensor(wx, wx, gp, ALU.mult))
            for k in range(4):
                g = gpq[:, :, 0:SW[k]]
                link(nc.vector.tensor_tensor(g, gsi[:, 8 * k:8 * k + 8].unsqueeze(2).broadcast_to([P, 8, SW[k]]),
                                             gsi[:, 8 * k:NP].unsqueeze(1).broadcast_to([P, 8, SW[k]]), ALU.mult))
                link(nc.vector.tensor_tensor(strip(k), strip(k), g.unsqueeze(1).broadcast_to([P, 4, 8, SW[k]]), ALU.mult))
            nc.vector.tensor_copy(gpq[:, 0, :], gsi[:, :]).then_inc(prep_dve, 1)
            def prepare_wlt():
                for c in range(RC):
                    dve.wait_ge(prep_mm, 8 + c)
                    link(nc.vector.tensor_reduce(wmean[:, c:c + 1], L[c % 2][:, :], AXX, ALU.add))
                    link(nc.vector.tensor_scalar(wmean[:, c:c + 1], wmean[:, c:c + 1], -1.0 / MAXD, None, ALU.mult))
                    nc.vector.tensor_scalar(wlt[:, c, :], L[c % 2][:, :], wmean[:, c:c + 1], None, ALU.add).then_inc(prep_dve, 1)

                for h in range(2):
                    nc.vector.memset(V[h][:, :, NP + 1:NP + 2], 1.0)

            def variance(tb, k, par):
                after(dve, y_squared, 8 * tb + k + 1)
                after(dve, stdy_done, 8 * tb + k - 1)
                nc.vector.tensor_reduce(var_y[k % 2][:, :], sq[k % 2][:, :, :], AXX, ALU.add).then_inc(vary_done, 1)

            def scale(tb, k, par):
                g, j2 = k // 2, k % 2
                after(dve, stdy_done, 8 * tb + k + 1)
                nc.vector.reciprocal(rstd_y[k % 2][:, :], std_y[k % 2][:, :]).then_inc(rstdy_done, 1)
                after(dve, rstdy_done, 8 * tb + k + 1)
                dst = V[par][:, :, :].rearrange("e (q m h) c -> e m q h c", q=NQ, h=2)[:, 4 * g:4 * g + 4, :, j2, 0:NP]
                nc.vector.tensor_tensor(dst, yb[k % 4][:, :, :].rearrange("e (m q) p -> e m q p", m=4),
                                        rstd_y[k % 2][:, :].rearrange("e (m q) -> e m q", m=4).unsqueeze(3).broadcast_to([P, 4, NQ, NP]),
                                        ALU.mult).then_inc(y_scaled, 1)

            def slot(i, s, live):
                t = TPG * i + s
                tb = t - 1
                A, B, C = live
                for k in range(PIECES):
                    yield k
                    if B:
                        if k == 0:
                            after(dve, gram_done, 4 * (tb - 1))
                            gx = i if s == 1 else i - 1
                            after(dve, x_ready, gx + 1)
                            nc.vector.tensor_copy(V[(s + 1) % 2][:, :, NP].rearrange("e (q j) -> e q j", q=NQ),
                                                  xt[:, :, (s + 1) % 2, :]).then_inc(x_in_v, 1)
                    if A and k == 4:
                        after(dve, stdn_done, t + 1)
                        nc.vector.reciprocal(rstd_n[:, :], std_n[:, :]).then_inc(rstdn_done, 1)
                        after(dve, rstdn_done, t + 1)
                        after(dve, nrm_stored[s], 16 * i)
                        nc.vector.tensor_tensor(nrm[s][:, :, :], emb[s][:, :, :], rstd_n[:, :].unsqueeze(2).broadcast_to([P, NF, D]),
                                                ALU.mult).then_inc(nrm_ready, 1)
                    at = lagging(i, s, k, 1)
                    if at:
                        u, n, _ = at
                        after(dve, proj_done, 8 * u + n + 1)
                        after(dve, y_scaled, 8 * u + n - 3)
                        nc.vector.tensor_tensor(yb[n % 4][:, :, :], b_y[n % 2][:, :].rearrange("e (s p) -> e s p", p=NP),
                                                bias_y[:, :].unsqueeze(1).broadcast_to([P, 16, NP]), ALU.add).then_inc(y_biased, 1)
                    at = lagging(i, s, k, 2)
                    if at:
                        variance(*at)
                    if A and k < 4:
                        c0, c1 = BATCHES[k][0], BATCHES[k][-1] + 1
                        n0, n1 = 2 * c0, 2 * c1
                        after(dve, gw_done, 4 * t + k + 1)
                        after(dve, varn_done, 4 * t + k - 1)
                        nc.vector.tensor_tensor(prod[k % 2][:, 0:n1 - n0, :], b_g[:, 0:(n1 - n0) * D].rearrange("p (n d) -> p n d", d=D),
                                                emb[s][:, n0:n1, :], ALU.mult).then_inc(prod_done, 1)
                        after(dve, prod_done, 4 * t + k + 1)
                        nc.vector.tensor_reduce(var_n[:, n0:n1], prod[k % 2][:, 0:n1 - n0, :], AXX, ALU.add).then_inc(varn_done, 1)
                    if A and k == 3:
                        after(dve, varn_done, 4 * t + 4)
                        nc.vector.tensor_scalar(var_m[:, :], var_n[:, :], 0.0, None, ALU.max).then_inc(varm_done, 1)
                    at = lagging(i, s, k, 3)
                    if at:
                        scale(*at)

            def body(i):
                live, front, back = stages(i)
                g = i - LAG
                for s in range(TPG):
                    for k in slot(i, s, live[s]):
                        p = PIECES * s + k
                        if front and p == 5:
                            after(dve, x_std, i + 1)
                            nc.vector.reciprocal(rx[:, :], sdx[:, :]).then_inc(x_step, 1)
                            after(dve, x_step, 2 * i + 1)
                            nc.vector.tensor_tensor(xn[:, :], L[0][:, 0:GB], rx[:, :], ALU.mult).then_inc(x_step, 1)
                            after(dve, x_step, 2 * i + 2)
                            after(dve, x_in_v, 2 * i)
                            nc.vector.tensor_scalar(xt[:, :, :, :].rearrange("p q t j -> p (q t j)"), xn[:, :], gd[:, 0:1], bd[:, 0:1],
                                                    ALU.mult, ALU.add).then_inc(x_ready, 1)
                        if back and p == 10:
                            after(dve, o_std, g + 1)
                            nc.vector.reciprocal(ro[:, :], sdo[:, :]).then_inc(o_rstd, 1)
                            after(dve, o_rstd, g + 1)
                            after(dve, o_copied, 2 * (g + 1))
                            after(dve, h1_done, 2 * g)
                            nc.vector.tensor_tensor(z[:, :, :], o_sb[:, 0:3, :], ro[:, :].unsqueeze(1).broadcast_to([P, 3, GB]), ALU.mult
                                                    ).then_inc(z_ready, 1)
                    if isinstance(i, int) and i == 0 and s == 0:
                        prepare_wlt()

            iterations(dve, body)


_NAMES = (["r_dense_t", "ids"] + [f"tbl_{f}" for f in range(NF)] + ["W_top1", "b_top1", "W_top2", "b_top2", "W_top3"]
          + [f"L0_rec_{n}" for n in ("Wd", "gd", "bd", "Ws", "gs", "bs", "Wsi", "gsi", "bsi", "Wl", "gl", "bl")])


def kernel(**inputs):
    import numpy as np
    import concourse.bacc as bacc
    from concourse.bass_utils import run_bass_kernel_spmd

    nc = bacc.Bacc("TRN2", target_bir_lowering=False, num_devices=1)
    arrays, aps = {}, {}
    for name in _NAMES:
        x = np.ascontiguousarray(inputs[name])
        arrays[f"in_{name}"] = x
        aps[name] = nc.dram_tensor(f"in_{name}", x.shape, mybir.dt.from_np(x.dtype), kind="ExternalInput").ap()
    out = nc.dram_tensor("out_y", (inputs["ids"].shape[0], 1), FP32, kind="ExternalOutput").ap()
    tower(nc, aps, out)
    result = run_bass_kernel_spmd(nc, [arrays], core_ids=[0])
    return result.results[0]["out_y"]
```
